# Optimizing a Trainium2 kernel written in Bass

```python
import numpy as np
import jax
import jax.numpy as jnp

def _softmax(x, axis=-1):
    return jax.nn.softmax(x, axis=axis)

def _gelu(x):
    return jax.nn.gelu(x, approximate=True)

def _silu(x):
    return jax.nn.silu(x)

def _sigmoid(x):
    return jax.nn.sigmoid(x)

def _layernorm(x, axis=-1, eps=1e-05):
    m = jnp.mean(x, axis=axis, keepdims=True)
    v = jnp.var(x, axis=axis, keepdims=True)
    return (x - m) / jnp.sqrt(v + eps)

def _scatter_add(tgt, idx, src, axis=0):
    return tgt.at[idx].add(src)

def _segment_sum(src, seg, n):
    return jax.ops.segment_sum(src, seg, n)
kernel_name = 'mk_dlrm_tower_d1_rec_r8_7ae8a9'

def setup_inputs(seed: int=0):
    np.random.seed(seed)
    _w = jnp.asarray

    def _rec_inputs():
        import jax
        import jax.numpy as jnp
        _tk = jax.random.key(seed)
        dense_ctx = jax.random.normal(jax.random.fold_in(_tk, 190), (512, 16), jnp.float32)
        ids = jnp.stack([jax.random.randint(jax.random.fold_in(_tk, 200 + f), (512,), 0, v, jnp.int32) for f, v in enumerate([1250, 1000, 1000, 12500, 12500, 125000, 12500, 125000, 1250, 1000, 1000, 1000, 125000, 125000, 12500, 1250, 1000, 125000, 1000, 1000, 1000, 125000, 12500, 125000, 12500, 12500])], axis=1)
        tbl_0 = 0.05 * jax.random.normal(jax.random.fold_in(_tk, 500 + 0), (1250, 32), jnp.float32)
        tbl_1 = 0.05 * jax.random.normal(jax.random.fold_in(_tk, 500 + 1), (1000, 32), jnp.float32)
        tbl_2 = 0.05 * jax.random.normal(jax.random.fold_in(_tk, 500 + 2), (1000, 32), jnp.float32)
        tbl_3 = 0.05 * jax.random.normal(jax.random.fold_in(_tk, 500 + 3), (12500, 32), jnp.float32)
        tbl_4 = 0.05 * jax.random.normal(jax.random.fold_in(_tk, 500 + 4), (12500, 32), jnp.float32)
        tbl_5 = 0.05 * jax.random.normal(jax.random.fold_in(_tk, 500 + 5), (125000, 32), jnp.float32)
        tbl_6 = 0.05 * jax.random.normal(jax.random.fold_in(_tk, 500 + 6), (12500, 32), jnp.float32)
        tbl_7 = 0.05 * jax.random.normal(jax.random.fold_in(_tk, 500 + 7), (125000, 32), jnp.float32)
        tbl_8 = 0.05 * jax.random.normal(jax.random.fold_in(_tk, 500 + 8), (1250, 32), jnp.float32)
        tbl_9 = 0.05 * jax.random.normal(jax.random.fold_in(_tk, 500 + 9), (1000, 32), jnp.float32)
        tbl_10 = 0.05 * jax.random.normal(jax.random.fold_in(_tk, 500 + 10), (1000, 32), jnp.float32)
        tbl_11 = 0.05 * jax.random.normal(jax.random.fold_in(_tk, 500 + 11), (1000, 32), jnp.float32)
        tbl_12 = 0.05 * jax.random.normal(jax.random.fold_in(_tk, 500 + 12), (125000, 32), jnp.float32)
        tbl_13 = 0.05 * jax.random.normal(jax.random.fold_in(_tk, 500 + 13), (125000, 32), jnp.float32)
        tbl_14 = 0.05 * jax.random.normal(jax.random.fold_in(_tk, 500 + 14), (12500, 32), jnp.float32)
        tbl_15 = 0.05 * jax.random.normal(jax.random.fold_in(_tk, 500 + 15), (1250, 32), jnp.float32)
        tbl_16 = 0.05 * jax.random.normal(jax.random.fold_in(_tk, 500 + 16), (1000, 32), jnp.float32)
        tbl_17 = 0.05 * jax.random.normal(jax.random.fold_in(_tk, 500 + 17), (125000, 32), jnp.float32)
        tbl_18 = 0.05 * jax.random.normal(jax.random.fold_in(_tk, 500 + 18), (1000, 32), jnp.float32)
        tbl_19 = 0.05 * jax.random.normal(jax.random.fold_in(_tk, 500 + 19), (1000, 32), jnp.float32)
        tbl_20 = 0.05 * jax.random.normal(jax.random.fold_in(_tk, 500 + 20), (1000, 32), jnp.float32)
        tbl_21 = 0.05 * jax.random.normal(jax.random.fold_in(_tk, 500 + 21), (125000, 32), jnp.float32)
        tbl_22 = 0.05 * jax.random.normal(jax.random.fold_in(_tk, 500 + 22), (12500, 32), jnp.float32)
        tbl_23 = 0.05 * jax.random.normal(jax.random.fold_in(_tk, 500 + 23), (125000, 32), jnp.float32)
        tbl_24 = 0.05 * jax.random.normal(jax.random.fold_in(_tk, 500 + 24), (12500, 32), jnp.float32)
        tbl_25 = 0.05 * jax.random.normal(jax.random.fold_in(_tk, 500 + 25), (12500, 32), jnp.float32)
        _rk = jax.random.fold_in(_tk, 7)
        W_top1 = 0.0606339 * jax.random.normal(jax.random.fold_in(_tk, 801), (272, 512), jnp.float32)
        W_top2 = 0.0441942 * jax.random.normal(jax.random.fold_in(_tk, 802), (512, 256), jnp.float32)
        W_top3 = 0.0625 * jax.random.normal(jax.random.fold_in(_tk, 803), (256, 1), jnp.float32)
        b_top1 = jnp.zeros((512,), jnp.float32)
        b_top2 = jnp.zeros((256,), jnp.float32)
        return (dense_ctx, ids, tbl_0, tbl_1, tbl_2, tbl_3, tbl_4, tbl_5, tbl_6, tbl_7, tbl_8, tbl_9, tbl_10, tbl_11, tbl_12, tbl_13, tbl_14, tbl_15, tbl_16, tbl_17, tbl_18, tbl_19, tbl_20, tbl_21, tbl_22, tbl_23, tbl_24, tbl_25, W_top1, b_top1, W_top2, b_top2, W_top3)
    dense_ctx, ids, tbl_0, tbl_1, tbl_2, tbl_3, tbl_4, tbl_5, tbl_6, tbl_7, tbl_8, tbl_9, tbl_10, tbl_11, tbl_12, tbl_13, tbl_14, tbl_15, tbl_16, tbl_17, tbl_18, tbl_19, tbl_20, tbl_21, tbl_22, tbl_23, tbl_24, tbl_25, W_top1, b_top1, W_top2, b_top2, W_top3 = _rec_inputs()

    def _L0_rec_setup():
        import jax, jax.numpy as jnp
        import numpy as np
        M_FIELDS = 26
        H1 = 128
        H2 = 128
        BATCH = 256
        EMB_K = 32

        def _cin_layer(x_prev, x0, W, b):
            return jnp.einsum('bik,bjk,hij->bhk', x_prev, x0, W) + b[None, :, None]
        key = jax.random.key(seed)
        k0, k1, k2, k3, k4 = jax.random.split(key, 5)
        inputs = jax.random.normal(k0, (BATCH, M_FIELDS, EMB_K), dtype=jnp.float32)
        W1 = jax.random.normal(k1, (H1, M_FIELDS, M_FIELDS), dtype=jnp.float32) * 0.05
        b1 = jax.random.normal(k2, (H1,), dtype=jnp.float32) * 0.05
        W2 = jax.random.normal(k3, (H2, H1, M_FIELDS), dtype=jnp.float32) * 0.05
        b2 = jax.random.normal(k4, (H2,), dtype=jnp.float32) * 0.05
        return {'inputs': inputs, 'W1': W1, 'b1': b1, 'W2': W2, 'b2': b2}
    _L0_rec_all = _L0_rec_setup()
    _L0_rec_in = {k: v for k, v in _L0_rec_all.items() if k in ('W1', 'b1', 'W2', 'b2')}
    del _L0_rec_all
    return {'dense_ctx': dense_ctx, 'ids': ids, 'tbl_0': tbl_0, 'tbl_1': tbl_1, 'tbl_2': tbl_2, 'tbl_3': tbl_3, 'tbl_4': tbl_4, 'tbl_5': tbl_5, 'tbl_6': tbl_6, 'tbl_7': tbl_7, 'tbl_8': tbl_8, 'tbl_9': tbl_9, 'tbl_10': tbl_10, 'tbl_11': tbl_11, 'tbl_12': tbl_12, 'tbl_13': tbl_13, 'tbl_14': tbl_14, 'tbl_15': tbl_15, 'tbl_16': tbl_16, 'tbl_17': tbl_17, 'tbl_18': tbl_18, 'tbl_19': tbl_19, 'tbl_20': tbl_20, 'tbl_21': tbl_21, 'tbl_22': tbl_22, 'tbl_23': tbl_23, 'tbl_24': tbl_24, 'tbl_25': tbl_25, 'W_top1': W_top1, 'b_top1': b_top1, 'W_top2': W_top2, 'b_top2': b_top2, 'W_top3': W_top3, 'L0_rec_W1': _L0_rec_in['W1'], 'L0_rec_b1': _L0_rec_in['b1'], 'L0_rec_W2': _L0_rec_in['W2'], 'L0_rec_b2': _L0_rec_in['b2']}

def reference(dense_ctx, ids, tbl_0, tbl_1, tbl_2, tbl_3, tbl_4, tbl_5, tbl_6, tbl_7, tbl_8, tbl_9, tbl_10, tbl_11, tbl_12, tbl_13, tbl_14, tbl_15, tbl_16, tbl_17, tbl_18, tbl_19, tbl_20, tbl_21, tbl_22, tbl_23, tbl_24, tbl_25, W_top1, b_top1, W_top2, b_top2, W_top3, L0_rec_W1, L0_rec_b1, L0_rec_W2, L0_rec_b2):
    import jax
    import jax.numpy as jnp

    def _L0_rec_ref(inputs, W1, b1, W2, b2):
        import jax, jax.numpy as jnp
        import numpy as np
        M_FIELDS = 26
        H1 = 128
        H2 = 128
        BATCH = 256
        EMB_K = 32

        def _cin_layer(x_prev, x0, W, b):
            return jnp.einsum('bik,bjk,hij->bhk', x_prev, x0, W) + b[None, :, None]
        x1 = _cin_layer(inputs, inputs, W1, b1)
        x2 = _cin_layer(x1, inputs, W2, b2)
        res = jnp.concatenate([x1, x2], axis=1)
        return jnp.sum(res, axis=-1)
    e = jnp.stack([tbl_0[ids[:, 0]], tbl_1[ids[:, 1]], tbl_2[ids[:, 2]], tbl_3[ids[:, 3]], tbl_4[ids[:, 4]], tbl_5[ids[:, 5]], tbl_6[ids[:, 6]], tbl_7[ids[:, 7]], tbl_8[ids[:, 8]], tbl_9[ids[:, 9]], tbl_10[ids[:, 10]], tbl_11[ids[:, 11]], tbl_12[ids[:, 12]], tbl_13[ids[:, 13]], tbl_14[ids[:, 14]], tbl_15[ids[:, 15]], tbl_16[ids[:, 16]], tbl_17[ids[:, 17]], tbl_18[ids[:, 18]], tbl_19[ids[:, 19]], tbl_20[ids[:, 20]], tbl_21[ids[:, 21]], tbl_22[ids[:, 22]], tbl_23[ids[:, 23]], tbl_24[ids[:, 24]], tbl_25[ids[:, 25]]], axis=1)
    z = _L0_rec_ref(e, L0_rec_W1, L0_rec_b1, L0_rec_W2, L0_rec_b2)
    z = z.reshape(z.shape[0], -1)
    h = jnp.concatenate([z, dense_ctx], axis=1)
    h = jnp.maximum(h @ W_top1 + b_top1, 0.0)
    h = jnp.maximum(h @ W_top2 + b_top2, 0.0)
    y = h @ W_top3
    return y

_drawn_inputs = setup_inputs


def setup_inputs(seed=0):
    import zlib

    import numpy as np

    out = dict(_drawn_inputs(seed))
    spreads = {'b_top1': (0.0, 2.0), 'b_top2': (0.0, 0.8)}
    factors = {'tbl_0': 8.0,
     'tbl_1': 8.0,
     'tbl_2': 8.0,
     'tbl_3': 8.0,
     'tbl_4': 8.0,
     'tbl_5': 8.0,
     'tbl_6': 8.0,
     'tbl_7': 8.0,
     'tbl_8': 8.0,
     'tbl_9': 8.0,
     'tbl_10': 8.0,
     'tbl_11': 8.0,
     'tbl_12': 8.0,
     'tbl_13': 8.0,
     'tbl_14': 8.0,
     'tbl_15': 8.0,
     'tbl_16': 8.0,
     'tbl_17': 8.0,
     'tbl_18': 8.0,
     'tbl_19': 8.0,
     'tbl_20': 8.0,
     'tbl_21': 7.701,
     'tbl_22': 8.0,
     'tbl_23': 8.0,
     'tbl_24': 8.0,
     'tbl_25': 8.0,
     'L0_rec_W1': 8.0,
     'L0_rec_W2': 4.119,
     'dense_ctx': 5.77}
    for name, (base, spread) in spreads.items():
        noise = np.random.default_rng([zlib.crc32(name.encode()), seed]).standard_normal(out[name].shape)
        drawn = base * np.exp(spread * noise) if base else spread * noise
        out[name] = jnp.asarray(drawn.astype(out[name].dtype))
    for name, factor in factors.items():
        out[name] = (out[name] * factor).astype(out[name].dtype)
    return out
```

```python
import concourse.bass as bass
from concourse import mybir
from contextlib import ExitStack

P = 128
BATCH, FIELDS, EMB, HID = 512, 26, 32, 128
DENSE, TOP1, TOP2 = 16, 512, 256
TILES = BATCH // P
QUADS = P // EMB
STEPS = P // QUADS
LO = 13


def tri(m):
    return m * (m + 1) // 2


PAIRS = 3 * P
LINEAR = tri(FIELDS)
B_FIRST, C_FIRST = 15, 22
EARLY = 16
LATE = FIELDS + 1 - B_FIRST
A_LATE, C_LATE = FIELDS + 1 - EARLY, FIELDS + 1 - C_FIRST
SLOTS = EARLY + A_LATE + C_LATE + LATE
A_ONE = FIELDS
C_0 = A_ONE + 1
C_ONE = C_0 + C_LATE - 1
B_0 = C_ONE + 1
B_ONE = B_0 + LATE - 1
WSLOTS = SLOTS + 1
C_Z1 = SLOTS
BAND0 = LO * LO
BANDS = BAND0 + (FIELDS - LO) * FIELDS
FW = BANDS + 1

GROUPS = [(0, 7), (7, 16), (16, 20), (20, 23), (23, 25), (25, 26)]
NG = len(GROUPS)
STEPS_BANK = 8
BANKS = STEPS // STEPS_BANK


def row_pieces(m, a0, a1):
    out, a = [], a0
    while a < a1:
        r = tri(m) + a
        n = min(a1 - a, P - r % P)
        out.append((r // P, r % P, a, n))
        a += n
    return out


def slot(chunk, single):
    return single if chunk == 0 else (B_0 + single - B_FIRST if chunk == 1 else C_0 + single - C_FIRST)


def program(nc, ids, tables, dense, W1, b1, W2, b2, Wt1, bt1, Wt2, bt2, Wt3, y):
    f32, i32 = mybir.dt.float32, mybir.dt.int32
    ALU, ACT = mybir.AluOpType, mybir.ActivationFunctionType
    ctx = ExitStack()
    with ctx:
        def sb(name, shape, dt=f32):
            return ctx.enter_context(nc.sbuf_tensor(name, shape, dt))

        def ps(name):
            return ctx.enter_context(nc.psum_tensor(name, [P, 512], f32))

        def sem(name):
            return ctx.enter_context(nc.semaphore(name))

        idx = sb("idx", [P, TILES, FIELDS], i32)
        rows = sb("rows", [P, TILES, FIELDS * EMB])
        eT = sb("eT", [P, STEPS, FIELDS])
        pairs = sb("pairs", [P, STEPS, PAIRS])
        e_early = sb("e_early", [P, STEPS, EARLY, QUADS])
        e_late = sb("e_late", [P, STEPS, LATE, QUADS])
        region1 = sb("region1", [P, FIELDS * FW])
        F = region1[:, :].rearrange("p (j n) -> p j n", n=FW)
        WT = region1[:, 0:WSLOTS * P].rearrange("p (s h) -> p s h", h=P)
        region2 = sb("region2", [P, WSLOTS * P])
        w2 = region2[:, 0:HID * FIELDS].rearrange("p (i j) -> p i j", j=FIELDS)
        wsym = region2[:, :].rearrange("p (s r) -> p s r", r=P)
        region3 = sb("region3", [P, SLOTS * P])
        w2T = region3[:, 0:FIELDS * P].rearrange("p (j h) -> p j h", h=P)
        T = region3[:, :].rearrange("p (s n) -> p s n", n=P)
        w1 = sb("w1", [P, FIELDS, FIELDS])
        S = sb("S", [P, FW])
        ident = sb("ident", [P, P])
        wt1 = sb("wt1", [P, 2, TOP1])
        wt1d = sb("wt1d", [DENSE, TOP1])
        wt2 = sb("wt2", [P, TOP1 // P, TOP2])
        wt3 = sb("wt3", [P, TOP2 // P])
        bias = sb("bias", [P, 8])
        bias_k = sb("bias_k", [P, 2])
        dense_rows = sb("dense_rows", [P, TILES, DENSE])
        denseT = sb("denseT", [DENSE, TILES, STEPS, QUADS])
        z = sb("z", [P, 2, P])
        h1 = sb("h1", [P, TOP1 // P, P])
        h2 = sb("h2", [P, TOP2 // P, P])
        yrow = sb("yrow", [1, TILES, QUADS, STEPS])

        p_early = [ps("p_early0"), ps("p_early1")]
        p_late = [ps("p_late0"), ps("p_late1")]
        p_z2, p_h1, p_x, p_w = ps("p_z2"), ps("p_h1"), ps("p_x"), ps("p_w")
        p_f = [p_late[0], p_late[1], p_z2, p_h1]
        p_wt = [p_w, p_x]

        ids_in, w1_in, w2_in, small_in, dense_in, top_in = map(
            sem, ("ids_in", "w1_in", "w2_in", "small_in", "dense_in", "top_in"))
        field_in = [[sem(f"field_in{t}_{g}") for g in range(NG)] for t in range(TILES)]
        ident_zero, ident_ready, static_ready = sem("ident_zero"), sem("ident_ready"), sem("static_ready")
        dense_t, dense_saved = sem("dense_t"), sem("dense_saved")
        w2t_done, w2t_saved = sem("w2t_done"), sem("w2t_saved")
        s_sum, s_ready = sem("s_sum"), sem("s_ready")
        f_done, f_saved = sem("f_done"), sem("f_saved")
        wsym_zero, wsym_part, wsym_base, wsym_sum, wsym_ready = map(
            sem, ("wsym_zero", "wsym_part", "wsym_base", "wsym_sum", "wsym_ready"))
        wt_done, wt_saved = sem("wt_done"), sem("wt_saved")
        et_ready, pairs_ready, singles_ready = sem("et_ready"), sem("pairs_ready"), sem("singles_ready")
        early_done, early_saved, late_done, late_saved = map(
            sem, ("early_done", "early_saved", "late_done", "late_saved"))
        ze_done, z1_done, z2_done, z_saved = map(sem, ("ze_done", "z1_done", "z2_done", "z_saved"))
        h1_done, h1_saved, h2_done, h2_saved, y_done, y_saved = map(
            sem, ("h1_done", "h1_saved", "h2_done", "h2_saved", "y_done", "y_saved"))
        bias_ready, out_done = sem("bias_ready"), sem("out_done")

        W2T_BANKS = -(-FIELDS // 4)
        WT_BANKS = -(-WSLOTS // 4)
        SMALL = 5

        block = ctx.enter_context(nc.Block())

        @block.sync
        def _(sp):
            sp.dma_start(idx[:, :, :], ids.rearrange("(t p) f -> p t f", p=P)).then_inc(ids_in, 16)
            sp.dma_start(region2[:, 0:HID * FIELDS], W2.rearrange("h i j -> h (i j)")).then_inc(w2_in, 16)
            sp.dma_start(wt1[:, :, :], Wt1[0:2 * P, :].rearrange("(c p) n -> p c n", p=P)).then_inc(top_in, 16)
            sp.dma_start(wt1d[:, :], Wt1[2 * P:2 * P + DENSE, :]).then_inc(top_in, 16)
            sp.dma_start(wt2[:, :, :], Wt2.rearrange("(c p) n -> p c n", p=P)).then_inc(top_in, 16)
            sp.dma_start(wt3[:, :], Wt3.rearrange("(c p) o -> p (c o)", p=P),
                         allow_slow_non_contiguous=True).then_inc(top_in, 16)
            sp.wait_ge(y_saved, TILES)
            sp.dma_start(y.rearrange("b o -> o b"), yrow[:, :, :, :].rearrange("o t q s -> o (t q s)")
                         ).then_inc(out_done, 16)
            sp.wait_ge(out_done, 16)

        @block.gpsimd
        def _(pool):
            nc.gpsimd.memset(ident[:, :], 0.0).then_inc(ident_zero, 1)
            pool.wait_ge(ident_zero, 1)
            nc.gpsimd.affine_select(out=ident[:, :], in_=ident[:, :], compare_op=ALU.not_equal, fill=1.0,
                                    base=0, pattern=[[-1, P]], channel_multiplier=1).then_inc(ident_ready, 1)
            pool.wait_ge(ids_in, 16)
            for t in range(TILES):
                for g, (f0, f1) in enumerate(GROUPS):
                    for f in range(f0, f1):
                        pool.indirect_dma_start(
                            rows[:, t, f * EMB:(f + 1) * EMB], None, tables[f],
                            bass.IndirectOffsetOnAxis(ap=idx[:, t, f:f + 1], axis=0),
                        ).then_inc(field_in[t][g], 16)

        @block.scalar
        def _(act):
            act.dma_start(w1[:, :, :], W1).then_inc(w1_in, 16)
            act.dma_start(S[:, BANDS:FW], b1.unsqueeze(1), allow_slow_non_contiguous=True).then_inc(small_in, 16)
            act.dma_start(bias[:, 0:1], b1.unsqueeze(1), allow_slow_non_contiguous=True).then_inc(small_in, 16)
            act.dma_start(bias[:, 1:2], b2.unsqueeze(1), allow_slow_non_contiguous=True).then_inc(small_in, 16)
            act.dma_start(bias[:, 2:6], bt1.rearrange("(c p) -> p c", p=P),
                          allow_slow_non_contiguous=True).then_inc(small_in, 16)
            act.dma_start(bias[:, 6:8], bt2.rearrange("(c p) -> p c", p=P),
                          allow_slow_non_contiguous=True).then_inc(small_in, 16)
            act.dma_start(dense_rows[:, :, :], dense.rearrange("(t p) d -> p t d", p=P)).then_inc(dense_in, 16)

            def singles(dst, f0, f1, s0):
                for q in range(QUADS):
                    part = slice(q * EMB, (q + 1) * EMB)
                    last = nc.scalar.copy(dst[part, :, s0:s0 + f1 - f0, q], eT[part, :, f0:f1])
                return last

            def singles_early(t):
                act.wait_ge(et_ready, NG * t + 2)
                if t == 0:
                    act.wait_ge(static_ready, 1)
                else:
                    act.wait_ge(early_done, BANKS * t)
                singles(e_early, 0, EARLY, 0).then_inc(singles_ready, 1)

            def singles_late(t):
                act.wait_ge(et_ready, NG * t + 4)
                if t:
                    act.wait_ge(late_done, 2 * BANKS * t)
                singles(e_late, B_FIRST, 23, 0)
                nc.scalar.copy(pairs[:, :, LINEAR:LINEAR + 23], eT[:, :, 0:23]).then_inc(singles_ready, 1)
                act.wait_ge(et_ready, NG * t + 6)
                singles(e_late, 23, FIELDS, 23 - B_FIRST)
                nc.scalar.copy(pairs[:, :, LINEAR + 23:LINEAR + FIELDS],
                               eT[:, :, 23:FIELDS]).then_inc(singles_ready, 1)

            def save_early(t):
                if t:
                    act.wait_ge(ze_done, t)
                for i in range(BANKS):
                    act.wait_ge(early_done, BANKS * t + i + 1)
                    n = i * STEPS_BANK * QUADS
                    nc.scalar.copy(
                        T[:, 0:EARLY, n:n + STEPS_BANK * QUADS].rearrange("p s (b q) -> p s b q", q=QUADS),
                        p_early[i % 2][:, :].rearrange("p (b s q) -> p s b q", b=STEPS_BANK, q=QUADS),
                    ).then_inc(early_saved, 1)

            def save_late(t):
                if t:
                    act.wait_ge(z2_done, t)
                for i in range(2 * BANKS):
                    act.wait_ge(late_done, 2 * BANKS * t + i + 1)
                    n = i % BANKS * STEPS_BANK * QUADS
                    s0, ns = (EARLY, A_LATE + C_LATE) if i < BANKS else (B_0, LATE)
                    nc.scalar.copy(
                        T[:, s0:s0 + ns, n:n + STEPS_BANK * QUADS].rearrange("p s (b q) -> p s b q", q=QUADS),
                        p_late[i % 2][:, 0:STEPS_BANK * ns * QUADS].rearrange(
                            "p (b s q) -> p s b q", b=STEPS_BANK, q=QUADS),
                    ).then_inc(late_saved, 1)

            def mlp(t):
                act.wait_ge(bias_ready, 1)
                if t:
                    act.wait_ge(h1_done, t)
                act.wait_ge(z1_done, t + 1)
                nc.scalar.activation(z[:, 0, :], p_x[:, 0:P], ACT.Identity, bias=bias_k[:, 0:1]).then_inc(z_saved, 1)
                act.wait_ge(z2_done, t + 1)
                nc.scalar.activation(z[:, 1, :], p_z2[:, 0:P], ACT.Identity, bias=bias_k[:, 1:2]).then_inc(z_saved, 1)
                act.wait_ge(h1_done, t + 1)
                if t:
                    act.wait_ge(h2_done, t)
                for c in range(TOP1 // P):
                    last = nc.scalar.activation(h1[:, c, :], p_h1[:, c * P:(c + 1) * P], ACT.Relu,
                                                bias=bias[:, 2 + c:3 + c])
                last.then_inc(h1_saved, 1)
                act.wait_ge(h2_done, t + 1)
                if t:
                    act.wait_ge(y_done, t)
                for c in range(TOP2 // P):
                    last = nc.scalar.activation(h2[:, c, :], p_x[:, (1 + c) * P:(2 + c) * P], ACT.Relu,
                                                bias=bias[:, 6 + c:7 + c])
                last.then_inc(h2_saved, 1)
                act.wait_ge(y_done, t + 1)
                nc.scalar.copy(yrow[0:1, t, :, :],
                               p_x[0:1, 3 * P:4 * P].rearrange("o (s q) -> o q s", q=QUADS)).then_inc(y_saved, 1)

            for i in range(W2T_BANKS):
                n = min(4, FIELDS - 4 * i)
                act.wait_ge(w2t_done, i + 1)
                nc.scalar.copy(w2T[:, 4 * i:4 * i + n, :],
                               p_early[i % 2][:, 0:n * P].rearrange("p (j h) -> p j h", h=P)).then_inc(w2t_saved, 1)
            act.wait_ge(dense_t, 1)
            nc.scalar.copy(denseT[:, :, :, :],
                           p_x[0:DENSE, :].rearrange("d (t q s) -> d t s q", t=TILES, q=QUADS)).then_inc(dense_saved, 1)
            for j in range(FIELDS):
                act.wait_ge(f_done, j + 1)
                nc.scalar.copy(F[:, j, :], p_f[j % 4][:, 0:FW]).then_inc(f_saved, 1)
                if j == FIELDS // 2:
                    singles_early(0)
            act.wait_ge(wsym_zero, 1)
            act.wait_ge(f_saved, FIELDS)
            for m in range(FIELDS):
                for chunk, col, a, n in row_pieces(m, 0, m + 1):
                    src = m * LO + a if m < LO else BAND0 + (m - LO) * FIELDS + a
                    nc.scalar.copy(wsym[:, slot(chunk, m), col:col + n], F[:, m, src:src + n])
            nc.scalar.copy(wsym[:, C_ONE, LINEAR % P:LINEAR % P + FIELDS], F[:, :, BANDS]).then_inc(wsym_base, 1)
            for m in range(FIELDS):
                for chunk, col, a, n in row_pieces(m, 0, m + 1):
                    src = m * LO + a if m < LO else BAND0 + (m - LO) * FIELDS + a
                    last = nc.scalar.copy(wsym[:, (A_ONE, B_ONE, C_Z1)[chunk], col:col + n], S[:, src:src + n])
            last.then_inc(wsym_base, 1)
            save_early(0)
            singles_late(0)
            save_late(0)
            act.wait_ge(wsym_ready, 1)
            for i in range(WT_BANKS):
                n = min(4, WSLOTS - 4 * i)
                act.wait_ge(wt_done, i + 1)
                nc.scalar.copy(WT[:, 4 * i:4 * i + n, :],
                               p_wt[i % 2][:, 0:n * P].rearrange("p (s h) -> p s h", h=P)).then_inc(wt_saved, 1)
            mlp(0)
            for t in range(1, TILES):
                singles_early(t)
                save_early(t)
                singles_late(t)
                save_late(t)
                mlp(t)

        @block.vector
        def _(dve):
            nc.vector.memset(e_early[:, :, :, :], 0.0)
            nc.vector.memset(e_late[:, :, :, :], 0.0).then_inc(s_sum, 1)
            nc.vector.memset(pairs[:, :, LINEAR + FIELDS:PAIRS], 0.0)
            dve.wait_ge(s_sum, 1)
            for q in range(QUADS):
                last = nc.vector.memset(e_late[q * EMB:(q + 1) * EMB, :, LATE - 1, q], 1.0)
            last.then_inc(static_ready, 1)
            dve.wait_ge(w1_in, 16)
            nc.vector.tensor_tensor(
                S[:, 0:BAND0].rearrange("p (m l) -> p m l", l=LO), w1[:, 0:LO, 0:LO],
                w1[:, 0:LO, 0:LO].rearrange("p l m -> p m l"), ALU.add)
            nc.vector.tensor_tensor(
                S[:, BAND0:BANDS].rearrange("p (m l) -> p m l", l=FIELDS), w1[:, LO:FIELDS, :],
                w1[:, :, LO:FIELDS].rearrange("p l m -> p m l"), ALU.add).then_inc(s_sum, 1)
            dve.wait_ge(s_sum, 2)
            w1f = w1[:, :, :].rearrange("p l m -> p (l m)")
            nc.vector.tensor_copy(S[:, 0:BAND0:LO + 1], w1f[:, 0:LO * FIELDS:FIELDS + 1])
            nc.vector.tensor_copy(S[:, BAND0 + LO:BANDS:FIELDS + 1],
                                  w1f[:, LO * (FIELDS + 1)::FIELDS + 1]).then_inc(s_ready, 1)
            dve.wait_ge(small_in, 16 * SMALL)
            nc.vector.tensor_scalar(bias_k[:, :], bias[:, 0:2], float(EMB), None, ALU.mult).then_inc(bias_ready, 1)
            dve.wait_ge(w2t_done, W2T_BANKS)
            nc.vector.memset(region2[:, :], 0.0).then_inc(wsym_zero, 1)

            def group(t, g):
                f0, f1 = GROUPS[g]
                dve.wait_ge(field_in[t][g], 16 * (f1 - f0))
                if t and g == 0:
                    dve.wait_ge(singles_ready, 3 * t)
                    dve.wait_ge(pairs_ready, NG * t)
                nc.vector.transpose(eT[:, :, f0:f1].rearrange("p b f -> p f b"),
                                    rows[:, t, f0 * EMB:f1 * EMB].rearrange("p (f k) -> p f k", k=EMB)
                                    ).then_inc(et_ready, 1)
                dve.wait_ge(et_ready, NG * t + g + 1)
                if t and g == 0:
                    dve.wait_ge(late_done, 2 * BANKS * (t - 1) + BANKS)
                if t and g == 1:
                    dve.wait_ge(late_done, 2 * BANKS * t)
                for m in range(f0, f1):
                    last = nc.vector.tensor_tensor(
                        pairs[:, :, tri(m):tri(m) + m + 1], eT[:, :, 0:m + 1],
                        eT[:, :, m:m + 1].to_broadcast([P, STEPS, m + 1]), ALU.mult)
                last.then_inc(pairs_ready, 1)

            def row(block_, m0, m1):
                if m1 <= LO:
                    return block_[..., 0:BAND0].rearrange("p (m l) -> p m l", l=LO)[:, m0:m1]
                return block_[..., BAND0:BANDS].rearrange("p (m l) -> p m l", l=FIELDS)[:, m0 - LO:m1 - LO]

            def bands(c0):
                return [(a, b) for a, b in ((c0, LO), (max(c0, LO), FIELDS)) if a < b]

            def symmetrize():
                dve.wait_ge(f_saved, FIELDS)
                for b in range(FIELDS - 1):
                    src = b * LO if b < LO else BAND0 + (b - LO) * FIELDS
                    for chunk, col, a, n in row_pieces(b, 0, b + 1):
                        for c0, c1 in bands(b + 1):
                            last = nc.vector.tensor_tensor(
                                wsym[:, slot(chunk, c0):slot(chunk, c1 - 1) + 1, col:col + n],
                                F[:, c0:c1, src + a:src + a + n],
                                row(F[:, b, :], c0, c1)[:, :, a:a + n], ALU.add)
                last.then_inc(wsym_part, 1)
                dve.wait_ge(wsym_part, 1)
                dve.wait_ge(wsym_base, 1)
                for b in range(1, FIELDS):
                    for chunk, col, a, n in row_pieces(b, 0, b):
                        for c0, c1 in bands(b):
                            dst = wsym[:, slot(chunk, c0):slot(chunk, c1 - 1) + 1, col:col + n]
                            if c1 <= LO:
                                part = F[:, a:a + n, c0 * LO:c1 * LO].rearrange("p a (c l) -> p c a l", l=LO)
                            else:
                                part = F[:, a:a + n, BAND0 + (c0 - LO) * FIELDS:BAND0 + (c1 - LO) * FIELDS
                                         ].rearrange("p a (c l) -> p c a l", l=FIELDS)
                            last = nc.vector.tensor_tensor(dst, dst, part[:, :, :, b], ALU.add)
                last.then_inc(wsym_ready, 1)

            for g in range(NG):
                if g == 3:
                    symmetrize()
                group(0, g)
            for t in range(1, TILES):
                for g in range(NG):
                    group(t, g)

        @block.tensor
        def _(pe):
            pe.wait_ge(ident_ready, 1)
            pe.wait_ge(w2_in, 16)
            for i in range(W2T_BANKS):
                if i >= 2:
                    pe.wait_ge(w2t_saved, i - 1)
                for j in range(4 * i, min(4 * i + 4, FIELDS)):
                    last = nc.tensor.transpose(p_early[i % 2][:, (j % 4) * P:(j % 4 + 1) * P], w2[:, :, j], ident[:, :])
                last.then_inc(w2t_done, 1)
            pe.wait_ge(dense_in, 16)
            for t in range(TILES):
                last = nc.tensor.matmul(p_x[0:DENSE, t * P:(t + 1) * P], dense_rows[:, t, :], ident[:, :],
                                        start=True, stop=True)
            last.then_inc(dense_t, 1)
            pe.wait_ge(s_ready, 1)
            pe.wait_ge(small_in, 16 * SMALL)
            for j in range(FIELDS):
                if j % 4 == 0:
                    pe.wait_ge(w2t_saved, j // 4 + 1)
                if j >= 4:
                    pe.wait_ge(f_saved, j - 3)
                nc.tensor.matmul(p_f[j % 4][:, 0:FW], w2T[:, j, :], S[:, :], start=True, stop=True).then_inc(f_done, 1)

            def t_early(t):
                pe.wait_ge(pairs_ready, NG * t + 2)
                pe.wait_ge(singles_ready, 3 * t + 1)
                for i in range(BANKS):
                    n = BANKS * t + i
                    if n == 0:
                        pe.wait_ge(w2t_saved, W2T_BANKS)
                    if n >= 2:
                        pe.wait_ge(early_saved, n - 1)
                    for b in range(STEPS_BANK):
                        s = i * STEPS_BANK + b
                        w = EARLY * QUADS
                        last = nc.tensor.matmul(p_early[i % 2][:, b * w:(b + 1) * w], pairs[:, s, 0:P],
                                                e_early[:, s, :, :], start=True, stop=True)
                    last.then_inc(early_done, 1)

            def t_late(t):
                pe.wait_ge(pairs_ready, NG * (t + 1))
                pe.wait_ge(singles_ready, 3 * (t + 1))
                if t == 0:
                    pe.wait_ge(f_saved, FIELDS)
                for i in range(2 * BANKS):
                    n = 2 * BANKS * t + i
                    if n >= 2:
                        pe.wait_ge(late_saved, n - 1)
                    bank = p_late[i % 2]
                    for b in range(STEPS_BANK):
                        s = i % BANKS * STEPS_BANK + b
                        if i < BANKS:
                            w = (A_LATE + C_LATE) * QUADS
                            nc.tensor.matmul(bank[:, b * w:b * w + A_LATE * QUADS], pairs[:, s, 0:P],
                                             e_late[:, s, EARLY - B_FIRST:LATE, :], start=True, stop=True)
                            last = nc.tensor.matmul(bank[:, b * w + A_LATE * QUADS:(b + 1) * w], pairs[:, s, 2 * P:3 * P],
                                                    e_late[:, s, C_FIRST - B_FIRST:LATE, :], start=True, stop=True)
                        else:
                            w = LATE * QUADS
                            last = nc.tensor.matmul(bank[:, b * w:(b + 1) * w], pairs[:, s, P:2 * P],
                                                    e_late[:, s, :, :], start=True, stop=True)
                    last.then_inc(late_done, 1)

            def z2_part(slots, first, final):
                for n, s in enumerate(slots):
                    last = nc.tensor.matmul(p_z2[:, 0:P], WT[:, s, :], T[:, s, :], start=(first and n == 0),
                                            stop=(final and n == len(slots) - 1))
                return last

            def z_early(t):
                pe.wait_ge(early_saved, BANKS * (t + 1))
                if t:
                    pe.wait_ge(z_saved, 2 * t)
                z2_part(range(EARLY), True, False).then_inc(ze_done, 1)

            def z_late(t):
                pe.wait_ge(late_saved, 2 * BANKS * (t + 1))
                if t:
                    pe.wait_ge(y_saved, t)
                for n, (w, s) in enumerate(((A_ONE, A_ONE), (B_ONE, B_ONE), (C_Z1, C_ONE))):
                    last = nc.tensor.matmul(p_x[:, 0:P], WT[:, w, :], T[:, s, :], start=(n == 0), stop=(n == 2))
                last.then_inc(z1_done, 1)
                z2_part([s for s in range(EARLY, SLOTS) if s not in (A_ONE, B_ONE)], False, True).then_inc(z2_done, 1)

            def mlp(t):
                if t == 0:
                    pe.wait_ge(top_in, 16 * 4)
                    pe.wait_ge(dense_saved, 1)
                pe.wait_ge(z_saved, 2 * (t + 1))
                if t:
                    pe.wait_ge(h1_saved, t)
                for c in range(TOP1 // P):
                    out, cols = p_h1[:, c * P:(c + 1) * P], slice(c * P, (c + 1) * P)
                    nc.tensor.matmul(out, wt1[:, 0, cols], z[:, 0, :], start=True, stop=False)
                    nc.tensor.matmul(out, wt1[:, 1, cols], z[:, 1, :], start=False, stop=False)
                    last = nc.tensor.matmul(out, wt1d[:, cols], denseT[:, t, :, :].rearrange("d s q -> d (s q)"),
                                            start=False, stop=True)
                last.then_inc(h1_done, 1)
                pe.wait_ge(h1_saved, t + 1)
                for c in range(TOP2 // P):
                    for k in range(TOP1 // P):
                        last = nc.tensor.matmul(p_x[:, (1 + c) * P:(2 + c) * P], wt2[:, k, c * P:(c + 1) * P], h1[:, k, :],
                                                start=(k == 0), stop=(k == TOP1 // P - 1))
                last.then_inc(h2_done, 1)
                pe.wait_ge(h2_saved, t + 1)
                for k in range(TOP2 // P):
                    last = nc.tensor.matmul(p_x[0:1, 3 * P:4 * P], wt3[:, k:k + 1], h2[:, k, :],
                                            start=(k == 0), stop=(k == TOP2 // P - 1))
                last.then_inc(y_done, 1)

            t_early(0)
            t_late(0)
            pe.wait_ge(wsym_ready, 1)
            pe.wait_ge(wsym_base, 2)
            for i in range(WT_BANKS):
                if i == 0:
                    pe.wait_ge(dense_saved, 1)
                if i >= 2:
                    pe.wait_ge(wt_saved, i - 1)
                for s in range(4 * i, min(4 * i + 4, WSLOTS)):
                    last = nc.tensor.transpose(p_wt[i % 2][:, (s % 4) * P:(s % 4 + 1) * P], wsym[:, s, :], ident[:, :])
                last.then_inc(wt_done, 1)
            pe.wait_ge(wt_saved, WT_BANKS)
            z_early(0)
            z_late(0)
            mlp(0)
            for t in range(1, TILES):
                t_early(t)
                z_early(t)
                t_late(t)
                z_late(t)
                mlp(t)


def kernel(**inputs):
    import numpy as np
    import concourse.bacc as bacc
    from concourse.bass_utils import run_bass_kernel_spmd

    nc = bacc.Bacc("TRN2", target_bir_lowering=False, num_devices=1)
    arrays = {}

    def dram(name):
        a = np.ascontiguousarray(inputs[name])
        arrays[f"in_{name}"] = a
        return nc.dram_tensor(f"in_{name}", a.shape, mybir.dt.from_np(a.dtype), kind="ExternalInput").ap()

    y = nc.dram_tensor("out_y", (BATCH, 1), mybir.dt.float32, kind="ExternalOutput").ap()
    program(nc, dram("ids"), [dram(f"tbl_{f}") for f in range(FIELDS)], dram("dense_ctx"),
            dram("L0_rec_W1"), dram("L0_rec_b1"), dram("L0_rec_W2"), dram("L0_rec_b2"),
            dram("W_top1"), dram("b_top1"), dram("W_top2"), dram("b_top2"), dram("W_top3"), y)
    result = run_bass_kernel_spmd(nc, [arrays], core_ids=[0])
    return result.results[0]["out_y"]
```

```python
import concourse.bass as bass
from concourse import mybir
from contextlib import ExitStack

P = 128
BATCH, FIELDS, EMB, HID = 512, 26, 32, 128
DENSE, TOP1, TOP2 = 16, 512, 256
TILES = BATCH // P
QUADS = P // EMB
STEPS = P // QUADS


def tri(m):
    return m * (m + 1) // 2


XF, CUT = 18, 13
ONE = FIELDS
Y_ROW = tri(CUT)
ROWS = (Y_ROW + tri(FIELDS - XF), tri(XF) - tri(CUT) + FIELDS)
LIN = tri(XF) - tri(CUT)
PAIRS = sum(ROWS)
SINGLES = (FIELDS + 1, FIELDS + 1 - CUT)
SLOTS = sum(SINGLES)
W_LIN = FIELDS + FIELDS - CUT
W_ONE = W_LIN + 1
W_MIX = W_ONE + 2
WSLOTS = W_MIX + FIELDS - XF
LO = 13
BAND0 = LO * LO
BANDS = BAND0 + (FIELDS - LO) * FIELDS
FW = BANDS + 1

GROUPS = [(0, 13), (13, 18), (18, 26)]
NG = len(GROUPS)
BANK_STEPS = (4, 8)
TURNS = STEPS // BANK_STEPS[1]


def t_slot(chunk, single):
    return single if chunk == 0 else SINGLES[0] + single - CUT


def w_slot(chunk, single):
    return single if chunk == 0 else FIELDS + single - CUT


def pair_row(m):
    if m >= XF:
        return 0, Y_ROW + tri(m - XF)
    return (0, tri(m)) if m < CUT else (1, tri(m) - tri(CUT))


def band_row(m):
    return m * LO if m < LO else BAND0 + (m - LO) * FIELDS


def program(nc, ids, tables, dense, W1, b1, W2, b2, Wt1, bt1, Wt2, bt2, Wt3, y):
    f32, i32 = mybir.dt.float32, mybir.dt.int32
    ALU, ACT = mybir.AluOpType, mybir.ActivationFunctionType
    ctx = ExitStack()
    with ctx:
        def sb(name, shape, dt=f32):
            return ctx.enter_context(nc.sbuf_tensor(name, shape, dt))

        def ps(name):
            return ctx.enter_context(nc.psum_tensor(name, [P, 512], f32))

        def sem(name):
            return ctx.enter_context(nc.semaphore(name))

        idx = sb("idx", [P, TILES, FIELDS], i32)
        rows = sb("rows", [P, TILES, FIELDS * EMB])
        eT = sb("eT", [P, STEPS, FIELDS])
        e_diag = sb("e_diag", [P, STEPS, FIELDS + 1, QUADS])
        region1 = sb("region1", [P, max(FIELDS * FW, WSLOTS * P + STEPS * PAIRS)])
        F = region1[:, 0:FIELDS * FW].rearrange("p (j n) -> p j n", n=FW)
        WT = region1[:, 0:WSLOTS * P].rearrange("p (s h) -> p s h", h=P)
        pairs = [sb("pairs", [P, STEPS, PAIRS])[:, :, :],
                 region1[:, WSLOTS * P:WSLOTS * P + STEPS * PAIRS].rearrange("p (s r) -> p s r", r=PAIRS)]
        region2 = sb("region2", [P, WSLOTS * P])
        w2 = region2[:, 0:HID * FIELDS].rearrange("p (i j) -> p i j", j=FIELDS)
        wsym = region2[:, :].rearrange("p (s r) -> p s r", r=P)
        region3 = sb("region3", [P, SLOTS * P])
        w2T = region3[:, 0:FIELDS * P].rearrange("p (j h) -> p j h", h=P)
        T = region3[:, :].rearrange("p (s n) -> p s n", n=P)
        w1 = sb("w1", [P, FIELDS, FIELDS])
        S = sb("S", [P, FW])
        ident = sb("ident", [P, P])
        wt1 = sb("wt1", [P, 2, TOP1])
        wt1d = sb("wt1d", [DENSE, TOP1])
        wt2 = sb("wt2", [P, TOP1 // P, TOP2])
        wt3 = sb("wt3", [P, TOP2 // P])
        bias = sb("bias", [P, 8])
        bias_k = sb("bias_k", [P, 2])
        dense_rows = sb("dense_rows", [P, TILES, DENSE])
        denseT = sb("denseT", [DENSE, TILES, STEPS, QUADS])
        z = sb("z", [P, 2, P])
        h1 = sb("h1", [P, TOP1 // P, P])
        h2 = sb("h2", [P, TOP2 // P, P])
        yrow = sb("yrow", [1, TILES, QUADS, STEPS])

        p_t = [[ps("p_t00"), ps("p_t01")], [ps("p_t10"), ps("p_t11")]]
        p_z2, p_h1, p_x, p_w = ps("p_z2"), ps("p_h1"), ps("p_x"), ps("p_w")
        p_w2 = [p_t[0][0], p_t[0][1], p_w, p_x]
        p_f = [p_t[1][0], p_t[1][1], p_z2, p_h1]
        p_wt = [p_w, p_x]

        ids_in, w1_in, w2_in, b1_in, small_in, dense_in, top_in = map(
            sem, ("ids_in", "w1_in", "w2_in", "b1_in", "small_in", "dense_in", "top_in"))
        field_in = [[sem(f"field_in{t}_{g}") for g in range(NG)] for t in range(TILES)]
        ident_zero, ident_ready = sem("ident_zero"), sem("ident_ready")
        diag_zero, static_ready = sem("diag_zero"), sem("static_ready")
        dense_t, dense_saved = sem("dense_t"), sem("dense_saved")
        w2t_done, w2t_saved = sem("w2t_done"), sem("w2t_saved")
        s_sum, s_ready = sem("s_sum"), sem("s_ready")
        f_done, f_saved = sem("f_done"), sem("f_saved")
        wsym_zero, wsym_part, wsym_base, wsym_ready = map(
            sem, ("wsym_zero", "wsym_part", "wsym_base", "wsym_ready"))
        wt_done = sem("wt_done")
        wt_saved = [sem("wt_saved_act"), sem("wt_saved_dve")]
        et_ready, pairs_ready, diag_ready = map(sem, ("et_ready", "pairs_ready", "diag_ready"))
        t_done = [sem("t0_done"), sem("t1_done")]
        t_saved = [sem("t0_saved"), sem("t1_saved")]
        z1_done, z2_done, z_saved = map(sem, ("z1_done", "z2_done", "z_saved"))
        h1_done, h1_saved, h2_done, h2_saved, y_done, y_saved = map(
            sem, ("h1_done", "h1_saved", "h2_done", "h2_saved", "y_done", "y_saved"))
        h1_saved_dve, h2_saved_dve = sem("h1_saved_dve"), sem("h2_saved_dve")
        bias_ready, out_done = sem("bias_ready"), sem("out_done")

        W2T_BANKS = -(-FIELDS // 4)
        WT_BANKS = -(-WSLOTS // 4)
        SMALL = 4
        LAST = TILES - 1
        BANKS = [STEPS // n for n in BANK_STEPS]

        def h1_sum(c):
            bank = (p_h1, p_w)[c // 2]
            return bank[:, c % 2 * P:(c % 2 + 1) * P]

        def h2_sum(c):
            return p_x[:, P:2 * P] if c == 0 else p_w[:, 3 * P:4 * P]

        block = ctx.enter_context(nc.Block())

        @block.sync
        def _(sp):
            sp.dma_start(idx[:, :, :], ids.rearrange("(t p) f -> p t f", p=P)).then_inc(ids_in, 16)
            sp.dma_start(region2[:, 0:HID * FIELDS], W2.rearrange("h i j -> h (i j)")).then_inc(w2_in, 16)
            sp.dma_start(wt1[:, :, :], Wt1[0:2 * P, :].rearrange("(c p) n -> p c n", p=P)).then_inc(top_in, 16)
            sp.dma_start(wt1d[:, :], Wt1[2 * P:2 * P + DENSE, :]).then_inc(top_in, 16)
            sp.dma_start(wt2[:, :, :], Wt2.rearrange("(c p) n -> p c n", p=P)).then_inc(top_in, 16)
            sp.dma_start(wt3[:, :], Wt3.rearrange("(c p) o -> p (c o)", p=P),
                         allow_slow_non_contiguous=True).then_inc(top_in, 16)
            sp.wait_ge(y_saved, TILES)
            sp.dma_start(y.rearrange("b o -> o b"), yrow[:, :, :, :].rearrange("o t q s -> o (t q s)")
                         ).then_inc(out_done, 16)
            sp.wait_ge(out_done, 16)

        @block.gpsimd
        def _(pool):
            nc.gpsimd.memset(ident[:, :], 0.0).then_inc(ident_zero, 1)
            pool.wait_ge(ident_zero, 1)
            nc.gpsimd.affine_select(out=ident[:, :], in_=ident[:, :], compare_op=ALU.not_equal, fill=1.0,
                                    base=0, pattern=[[-1, P]], channel_multiplier=1).then_inc(ident_ready, 1)
            pool.wait_ge(ids_in, 16)
            for t in range(TILES):
                for g, (f0, f1) in enumerate(GROUPS):
                    for f in range(f0, f1):
                        pool.indirect_dma_start(
                            rows[:, t, f * EMB:(f + 1) * EMB], None, tables[f],
                            bass.IndirectOffsetOnAxis(ap=idx[:, t, f:f + 1], axis=0),
                        ).then_inc(field_in[t][g], 16)

        @block.scalar
        def _(act):
            act.dma_start(S[:, BANDS:FW], b1.unsqueeze(1), allow_slow_non_contiguous=True).then_inc(b1_in, 16)
            act.dma_start(w1[:, :, :], W1).then_inc(w1_in, 16)
            act.dma_start(bias[:, 0:1], b1.unsqueeze(1), allow_slow_non_contiguous=True).then_inc(small_in, 16)
            act.dma_start(bias[:, 1:2], b2.unsqueeze(1), allow_slow_non_contiguous=True).then_inc(small_in, 16)
            act.dma_start(bias[:, 2:6], bt1.rearrange("(c p) -> p c", p=P),
                          allow_slow_non_contiguous=True).then_inc(small_in, 16)
            act.dma_start(bias[:, 6:8], bt2.rearrange("(c p) -> p c", p=P),
                          allow_slow_non_contiguous=True).then_inc(small_in, 16)
            act.dma_start(dense_rows[:, :, :], dense.rearrange("(t p) d -> p t d", p=P)).then_inc(dense_in, 16)

            def save_bank(t, chunk, i):
                n = BANKS[chunk] * t + i
                steps, ns = BANK_STEPS[chunk], SINGLES[chunk]
                col, s0 = i * steps * QUADS, t_slot(chunk, 0 if chunk == 0 else CUT)
                act.wait_ge(t_done[chunk], n + 1)
                nc.scalar.copy(
                    T[0:ROWS[chunk], s0:s0 + ns, col:col + steps * QUADS].rearrange("p s (b q) -> p s b q", q=QUADS),
                    p_t[chunk][i % 2][0:ROWS[chunk], 0:steps * ns * QUADS].rearrange(
                        "p (b s q) -> p s b q", b=steps, q=QUADS),
                ).then_inc(t_saved[chunk], 1)

            def save_turn(t, k):
                save_bank(t, 0, 2 * k)
                save_bank(t, 0, 2 * k + 1)
                save_bank(t, 1, k)

            def save_z(t):
                act.wait_ge(bias_ready, 1)
                if t:
                    act.wait_ge(h1_done, t)
                act.wait_ge(z1_done, t + 1)
                nc.scalar.activation(z[:, 0, :], p_x[:, 0:P], ACT.Identity, bias=bias_k[:, 0:1]).then_inc(z_saved, 1)
                act.wait_ge(z2_done, t + 1)
                nc.scalar.activation(z[:, 1, :], p_z2[:, 0:P], ACT.Identity, bias=bias_k[:, 1:2]).then_inc(z_saved, 1)

            def save_h1(t):
                act.wait_ge(h1_done, t + 1)
                if t:
                    act.wait_ge(h2_done, t)
                for c in range(TOP1 // P // (2 if t == LAST else 1)):
                    last = nc.scalar.activation(h1[:, c, :], h1_sum(c), ACT.Relu, bias=bias[:, 2 + c:3 + c])
                last.then_inc(h1_saved, 1)

            def save_h2(t):
                act.wait_ge(h2_done, t + 1)
                if t:
                    act.wait_ge(y_done, t)
                for c in range(TOP2 // P // (2 if t == LAST else 1)):
                    last = nc.scalar.activation(h2[:, c, :], h2_sum(c), ACT.Relu, bias=bias[:, 6 + c:7 + c])
                last.then_inc(h2_saved, 1)

            def save_y(t):
                act.wait_ge(y_done, t + 1)
                nc.scalar.copy(yrow[0:1, t, :, :],
                               p_x[0:1, 3 * P:4 * P].rearrange("o (s q) -> o q s", q=QUADS)).then_inc(y_saved, 1)

            def save_w2t(i):
                n = min(4, FIELDS - 4 * i)
                act.wait_ge(w2t_done, i + 1)
                nc.scalar.copy(w2T[:, 4 * i:4 * i + n, :],
                               p_w2[i % 4][:, 0:n * P].rearrange("p (j h) -> p j h", h=P)).then_inc(w2t_saved, 1)

            for i in range(W2T_BANKS):
                save_w2t(i)

            def base_weight(m):
                (chunk, r), a0 = pair_row(m), XF if m >= XF else 0
                return nc.scalar.copy(wsym[:, w_slot(chunk, m), r:r + m + 1 - a0],
                                      F[:, m, band_row(m) + a0:band_row(m) + m + 1])

            def z1_weight(m):
                (chunk, r), a0 = pair_row(m), XF if m >= XF else 0
                return nc.scalar.copy(wsym[:, W_ONE + chunk, r:r + m + 1 - a0],
                                      S[:, band_row(m) + a0:band_row(m) + m + 1])

            START = 12
            weights_left = list(range(FIELDS))
            for j in range(FIELDS):
                act.wait_ge(f_done, j + 1)
                nc.scalar.copy(F[:, j, :], p_f[j % 4][:, 0:FW]).then_inc(f_saved, 1)
                if j == START:
                    act.wait_ge(wsym_zero, 1)
                if j >= START:
                    act.wait_ge(f_saved, j)
                    for m in [m for m in weights_left if m < j][:3]:
                        weights_left.remove(m)
                        base_weight(m)
                        z1_weight(m)
            act.wait_ge(f_saved, FIELDS)
            for m in weights_left:
                base_weight(m)
                z1_weight(m)
            nc.scalar.copy(wsym[:, W_LIN, LIN:LIN + FIELDS], F[:, :, BANDS])
            nc.scalar.copy(wsym[:, W_MIX:WSLOTS, LIN:LIN + XF],
                           S[:, band_row(XF):BANDS].rearrange("p (m l) -> p m l", l=FIELDS)[:, :, 0:XF]
                           ).then_inc(wsym_base, 1)
            act.wait_ge(dense_t, 1)
            nc.scalar.copy(denseT[:, :, :, :],
                           p_x[0:DENSE, :].rearrange("d (t q s) -> d t s q", t=TILES, q=QUADS)).then_inc(dense_saved, 1)
            for k in range(TURNS):
                save_turn(0, k)
            act.wait_ge(wsym_ready, 1)
            for i in range(0, WT_BANKS, 2):
                n = min(4, WSLOTS - 4 * i)
                act.wait_ge(wt_done, i + 1)
                nc.scalar.copy(WT[0:ROWS[0], 4 * i:4 * i + n, :],
                               p_wt[0][0:ROWS[0], 0:n * P].rearrange("p (s h) -> p s h", h=P)).then_inc(wt_saved[0], 1)
            for t in range(1, TILES):
                save_z(t - 1)
                save_turn(t, 0)
                save_h1(t - 1)
                save_turn(t, 1)
                save_h2(t - 1)
                save_turn(t, 2)
                save_y(t - 1)
                save_turn(t, 3)
            save_z(TILES - 1)
            save_h1(TILES - 1)
            save_h2(TILES - 1)
            save_y(TILES - 1)

        @block.vector
        def _(dve):
            dve.wait_ge(w1_in, 16)
            nc.vector.tensor_tensor(
                S[:, 0:BAND0].rearrange("p (m l) -> p m l", l=LO), w1[:, 0:LO, 0:LO],
                w1[:, 0:LO, 0:LO].rearrange("p l m -> p m l"), ALU.add)
            nc.vector.tensor_tensor(
                S[:, BAND0:BANDS].rearrange("p (m l) -> p m l", l=FIELDS), w1[:, LO:FIELDS, :],
                w1[:, :, LO:FIELDS].rearrange("p l m -> p m l"), ALU.add).then_inc(s_sum, 1)
            dve.wait_ge(s_sum, 1)
            w1f = w1[:, :, :].rearrange("p l m -> p (l m)")
            nc.vector.tensor_copy(S[:, 0:BAND0:LO + 1], w1f[:, 0:LO * FIELDS:FIELDS + 1])
            nc.vector.tensor_copy(S[:, BAND0 + LO:BANDS:FIELDS + 1],
                                  w1f[:, LO * (FIELDS + 1)::FIELDS + 1]).then_inc(s_ready, 1)
            nc.vector.memset(e_diag[:, :, :, :], 0.0).then_inc(diag_zero, 1)
            dve.wait_ge(diag_zero, 1)
            for q in range(QUADS):
                last = nc.vector.memset(e_diag[q * EMB:(q + 1) * EMB, :, ONE, q], 1.0)
            last.then_inc(static_ready, 1)
            dve.wait_ge(small_in, 16 * SMALL)
            nc.vector.tensor_scalar(bias_k[:, :], bias[:, 0:2], float(EMB), None, ALU.mult).then_inc(bias_ready, 1)

            def group(t, g):
                f0, f1 = GROUPS[g]
                dve.wait_ge(field_in[t][g], 16 * (f1 - f0))
                if t and g == 0:
                    dve.wait_ge(diag_ready, t)
                nc.vector.transpose(eT[:, :, f0:f1].rearrange("p b f -> p f b"),
                                    rows[:, t, f0 * EMB:f1 * EMB].rearrange("p (f k) -> p f k", k=EMB)
                                    ).then_inc(et_ready, 1)
                dve.wait_ge(et_ready, NG * t + g + 1)
                if t == 1 and g == 0:
                    dve.wait_ge(wsym_ready, 1)
                if t >= 2 and g == 0:
                    dve.wait_ge(t_done[1], BANKS[1] * (t - 1))
                for m in range(f0, f1):
                    (chunk, r), a0 = pair_row(m), XF if m >= XF else 0
                    r += chunk * ROWS[0]
                    last = nc.vector.tensor_tensor(
                        pairs[t % 2][:, :, r:r + m + 1 - a0], eT[:, :, a0:m + 1],
                        eT[:, :, m:m + 1].to_broadcast([P, STEPS, m + 1 - a0]), ALU.mult)
                last.then_inc(pairs_ready, 1)

            def singles(t):
                if t:
                    dve.wait_ge(t_done[1], BANKS[1] * t)
                nc.vector.tensor_copy(pairs[t % 2][:, :, ROWS[0] + LIN:PAIRS], eT[:, :, :])
                for q in range(QUADS):
                    part = slice(q * EMB, (q + 1) * EMB)
                    last = nc.vector.tensor_copy(e_diag[part, :, 0:FIELDS, q], eT[part, :, :])
                last.then_inc(diag_ready, 1)

            def block_rows(block_, m0, m1):
                if m1 <= LO:
                    return block_[:, m0 * LO:m1 * LO].rearrange("p (m l) -> p m l", l=LO)
                return block_[:, band_row(m0):band_row(m0) + (m1 - m0) * FIELDS].rearrange("p (m l) -> p m l", l=FIELDS)

            def column(m0, m1, a0, a1, b):
                w = LO if m1 <= LO else FIELDS
                part = F[:, a0:a1, band_row(m0):band_row(m0) + (m1 - m0) * w]
                return part.rearrange("p a (m l) -> p m a l", l=w)[:, :, :, b]

            def bands(c0):
                return [(a, b) for a, b in ((c0, LO), (max(c0, LO), FIELDS)) if a < b]

            def weights(b):
                (chunk, r), a0 = pair_row(b), XF if b >= XF else 0
                return a0, lambda c0, c1, a1: wsym[:, w_slot(chunk, c0):w_slot(chunk, c1 - 1) + 1, r:r + a1 - a0]

            def symmetrize():
                dve.wait_ge(wsym_zero, 1)
                dve.wait_ge(f_saved, FIELDS)
                for b in range(FIELDS - 1):
                    a0, dst = weights(b)
                    src = band_row(b)
                    for c0, c1 in bands(b + 1):
                        nc.vector.tensor_tensor(dst(c0, c1, b + 1), F[:, c0:c1, src + a0:src + b + 1],
                                                block_rows(F[:, b, :], c0, c1)[:, :, a0:b + 1], ALU.add)
                for c in range(XF, FIELDS):
                    r = pair_row(c)[1]
                    src = band_row(c)
                    last = nc.vector.tensor_tensor(
                        wsym[:, 0:XF, r:r + c + 1 - XF], F[:, 0:XF, src + XF:src + c + 1],
                        F[:, XF:c + 1, src:src + XF].rearrange("p b a -> p a b"), ALU.add)
                last.then_inc(wsym_part, 1)
                dve.wait_ge(wsym_part, 1)
                dve.wait_ge(wsym_base, 1)
                for b in range(1, FIELDS):
                    a0, dst = weights(b)
                    if b > a0:
                        for c0, c1 in bands(b):
                            nc.vector.tensor_tensor(dst(c0, c1, b), dst(c0, c1, b), column(c0, c1, a0, b, b), ALU.add)
                for c in range(XF + 1, FIELDS):
                    r = pair_row(c)[1]
                    dst = wsym[:, 0:XF, r:r + c - XF]
                    last = nc.vector.tensor_tensor(
                        dst, dst, block_rows(F[:, c, :], XF, c)[:, :, 0:XF].rearrange("p b a -> p a b"), ALU.add)
                last.then_inc(wsym_ready, 1)

            dve.wait_ge(w2t_done, W2T_BANKS)
            nc.vector.memset(region2[:, :], 0.0).then_inc(wsym_zero, 1)
            for g in range(NG):
                group(0, g)
            singles(0)
            symmetrize()
            for i in range(1, WT_BANKS, 2):
                n = min(4, WSLOTS - 4 * i)
                dve.wait_ge(wt_done, i + 1)
                nc.vector.tensor_copy(WT[0:ROWS[0], 4 * i:4 * i + n, :],
                                      p_wt[1][0:ROWS[0], 0:n * P].rearrange("p (s h) -> p s h", h=P)
                                      ).then_inc(wt_saved[1], 1)
            for t in range(1, TILES):
                for g in range(NG):
                    group(t, g)
                singles(t)
            dve.wait_ge(h1_done, TILES)
            dve.wait_ge(h2_done, LAST)
            for c in (2, 3):
                last = nc.vector.tensor_scalar(h1[:, c, :], h1_sum(c), bias[:, 2 + c:3 + c], 0.0, ALU.add, ALU.max)
            last.then_inc(h1_saved_dve, 1)
            dve.wait_ge(h2_done, TILES)
            dve.wait_ge(y_done, LAST)
            nc.vector.tensor_scalar(h2[:, 1, :], h2_sum(1), bias[:, 7:8], 0.0, ALU.add, ALU.max).then_inc(h2_saved_dve, 1)

        @block.tensor
        def _(pe):
            pe.wait_ge(ident_ready, 1)
            pe.wait_ge(w2_in, 16)
            for i in range(W2T_BANKS):
                if i >= 4:
                    pe.wait_ge(w2t_saved, i - 3)
                for j in range(4 * i, min(4 * i + 4, FIELDS)):
                    last = nc.tensor.transpose(p_w2[i % 4][:, (j % 4) * P:(j % 4 + 1) * P], w2[:, :, j], ident[:, :])
                last.then_inc(w2t_done, 1)
            pe.wait_ge(s_ready, 1)
            pe.wait_ge(b1_in, 16)
            for j in range(FIELDS):
                if j % 4 == 0:
                    pe.wait_ge(w2t_saved, j // 4 + 1)
                if j >= 4:
                    pe.wait_ge(f_saved, j - 3)
                nc.tensor.matmul(p_f[j % 4][:, 0:FW], w2T[:, j, :], S[:, :], start=True, stop=True).then_inc(f_done, 1)
            pe.wait_ge(dense_in, 16)
            for t in range(TILES):
                last = nc.tensor.matmul(p_x[0:DENSE, t * P:(t + 1) * P], dense_rows[:, t, :], ident[:, :],
                                        start=True, stop=True)
            last.then_inc(dense_t, 1)

            def products(t, chunk, i):
                n = BANKS[chunk] * t + i
                if n >= 2:
                    pe.wait_ge(t_saved[chunk], n - 1)
                w, steps = SINGLES[chunk] * QUADS, BANK_STEPS[chunk]
                r0, s0 = chunk * ROWS[0], chunk * CUT
                for b in range(steps):
                    s = i * steps + b
                    last = nc.tensor.matmul(
                        p_t[chunk][i % 2][0:ROWS[chunk], b * w:(b + 1) * w], pairs[t % 2][:, s, r0:r0 + ROWS[chunk]],
                        e_diag[:, s, s0:FIELDS + 1, :].rearrange("p j q -> p (j q)"), start=True, stop=True)
                last.then_inc(t_done[chunk], 1)

            def turn(t, k):
                if k == 0:
                    pe.wait_ge(pairs_ready, NG * (t + 1))
                    pe.wait_ge(diag_ready, t + 1)
                    if t == 0:
                        pe.wait_ge(f_saved, FIELDS)
                products(t, 0, 2 * k)
                products(t, 0, 2 * k + 1)
                products(t, 1, k)

            def weighted(out, terms):
                for n, (w, s, chunk) in enumerate(terms):
                    last = nc.tensor.matmul(out, WT[0:ROWS[chunk], w, :], T[0:ROWS[chunk], s, :],
                                            start=(n == 0), stop=(n == len(terms) - 1))
                return last

            def z_sums(t):
                for chunk in (0, 1):
                    pe.wait_ge(t_saved[chunk], BANKS[chunk] * (t + 1))
                if t:
                    pe.wait_ge(y_saved, t)
                    pe.wait_ge(z_saved, 2 * t)
                weighted(p_x[:, 0:P],
                         [(W_ONE, t_slot(0, ONE), 0), (W_ONE + 1, t_slot(1, ONE), 1)]
                         + [(W_MIX + c - XF, t_slot(1, c), 1) for c in range(XF, FIELDS)]).then_inc(z1_done, 1)
                weighted(p_z2[:, 0:P],
                         [(w_slot(0, c), t_slot(0, c), 0) for c in range(FIELDS)]
                         + [(w_slot(1, c), t_slot(1, c), 1) for c in range(CUT, FIELDS)]
                         + [(W_LIN, t_slot(1, ONE), 1)]).then_inc(z2_done, 1)

            def h1_sums(t):
                if t == 0:
                    pe.wait_ge(top_in, 16 * 4)
                    pe.wait_ge(dense_saved, 1)
                if t:
                    pe.wait_ge(h1_saved, t)
                    pe.wait_ge(h2_saved, t)
                terms = [(wt1d[:, :], denseT[:, t, :, :].rearrange("d s q -> d (s q)")),
                         (wt1[:, 0, :], z[:, 0, :]), (wt1[:, 1, :], z[:, 1, :])]
                for n, (w, x) in enumerate(terms):
                    if n:
                        pe.wait_ge(z_saved, 2 * t + n)
                    for c in range(TOP1 // P):
                        last = nc.tensor.matmul(h1_sum(c), w[:, c * P:(c + 1) * P], x,
                                                start=(n == 0 and c % 2 == 0), stop=(n == 2), skip_group_check=True)
                last.then_inc(h1_done, 1)

            def h2_sums(t):
                pe.wait_ge(h1_saved, t + 1)
                if t == LAST:
                    pe.wait_ge(h1_saved_dve, 1)
                for c in range(TOP2 // P):
                    for k in range(TOP1 // P):
                        last = nc.tensor.matmul(h2_sum(c), wt2[:, k, c * P:(c + 1) * P], h1[:, k, :],
                                                start=(k == 0), stop=(k == TOP1 // P - 1))
                last.then_inc(h2_done, 1)

            def y_sums(t):
                pe.wait_ge(h2_saved, t + 1)
                if t == LAST:
                    pe.wait_ge(h2_saved_dve, 1)
                for k in range(TOP2 // P):
                    last = nc.tensor.matmul(p_x[0:1, 3 * P:4 * P], wt3[:, k:k + 1], h2[:, k, :],
                                            start=(k == 0), stop=(k == TOP2 // P - 1))
                last.then_inc(y_done, 1)

            for k in range(TURNS):
                turn(0, k)
            pe.wait_ge(wsym_ready, 1)
            pe.wait_ge(wsym_base, 1)
            pe.wait_ge(dense_saved, 1)
            for i in range(WT_BANKS):
                if i >= 2:
                    pe.wait_ge(wt_saved[i % 2], i // 2)
                for s in range(4 * i, min(4 * i + 4, WSLOTS)):
                    last = nc.tensor.transpose(p_wt[i % 2][0:ROWS[0], (s % 4) * P:(s % 4 + 1) * P],
                                               wsym[:, s, 0:ROWS[0]], ident[:, :])
                last.then_inc(wt_done, 1)
            pe.wait_ge(wt_saved[0], -(-WT_BANKS // 2))
            pe.wait_ge(wt_saved[1], WT_BANKS // 2)
            z_sums(0)
            for t in range(1, TILES):
                turn(t, 0)
                h1_sums(t - 1)
                turn(t, 1)
                h2_sums(t - 1)
                turn(t, 2)
                y_sums(t - 1)
                turn(t, 3)
                z_sums(t)
            h1_sums(TILES - 1)
            h2_sums(TILES - 1)
            y_sums(TILES - 1)


def kernel(**inputs):
    import numpy as np
    import concourse.bacc as bacc
    from concourse.bass_utils import run_bass_kernel_spmd

    nc = bacc.Bacc("TRN2", target_bir_lowering=False, num_devices=1)
    arrays = {}

    def dram(name):
        a = np.ascontiguousarray(inputs[name])
        arrays[f"in_{name}"] = a
        return nc.dram_tensor(f"in_{name}", a.shape, mybir.dt.from_np(a.dtype), kind="ExternalInput").ap()

    y = nc.dram_tensor("out_y", (BATCH, 1), mybir.dt.float32, kind="ExternalOutput").ap()
    program(nc, dram("ids"), [dram(f"tbl_{f}") for f in range(FIELDS)], dram("dense_ctx"),
            dram("L0_rec_W1"), dram("L0_rec_b1"), dram("L0_rec_W2"), dram("L0_rec_b2"),
            dram("W_top1"), dram("b_top1"), dram("W_top2"), dram("b_top2"), dram("W_top3"), y)
    result = run_bass_kernel_spmd(nc, [arrays], core_ids=[0])
    return result.results[0]["out_y"]
```
